# Optimizing a Trainium2 kernel written in Bass

```python
import numpy as np
import jax
import jax.numpy as jnp

def _softmax(x, axis=-1):
    return jax.nn.softmax(x, axis=axis)

def _gelu(x):
    return jax.nn.gelu(x, approximate=True)

def _silu(x):
    return jax.nn.silu(x)

def _sigmoid(x):
    return jax.nn.sigmoid(x)

def _layernorm(x, axis=-1, eps=1e-05):
    m = jnp.mean(x, axis=axis, keepdims=True)
    v = jnp.var(x, axis=axis, keepdims=True)
    return (x - m) / jnp.sqrt(v + eps)

def _scatter_add(tgt, idx, src, axis=0):
    return tgt.at[idx].add(src)

def _segment_sum(src, seg, n):
    return jax.ops.segment_sum(src, seg, n)
kernel_name = 'mk_gnn_resnorm_d4_gnn_r32_cb0625'

def setup_inputs(seed: int=0):
    np.random.seed(seed)
    _w = jnp.asarray

    def _rec_inputs():
        import jax
        import jax.numpy as jnp
        _gk = jax.random.key(seed)
        x = -0.0001006 + 1 * jax.random.normal(jax.random.fold_in(_gk, 1), (3125, 48), jnp.float32)
        _s = jax.random.randint(jax.random.fold_in(_gk, 2), (50000,), 0, 3125, jnp.int32)
        _d = jax.random.randint(jax.random.fold_in(_gk, 3), (50000,), 0, 3125, jnp.int32)
        _loop = jnp.arange(3125, dtype=jnp.int32)
        src = jnp.concatenate([_s, _d, _loop])
        dst = jnp.concatenate([_d, _s, _loop])
        _o = jnp.argsort(dst, stable=True)
        src = src[_o]
        dst = dst[_o]
        edge_attr_16 = 0.000196303 + 1.00016 * jax.random.normal(jax.random.fold_in(_gk, 12), (103125, 16), jnp.float32)
        edge_type_8 = jax.random.randint(jax.random.fold_in(_gk, 14), (103125,), 0, 8, jnp.int32)
        edge_weight1 = jax.random.uniform(jax.random.fold_in(_gk, 15), (103125, 1), jnp.float32, 0.0, 1)
        return (x, src, dst, edge_attr_16, edge_type_8, edge_weight1)
    x, src, dst, edge_attr_16, edge_type_8, edge_weight1 = _rec_inputs()

    def _L0_gnn_setup():
        import jax, jax.numpy as jnp
        import numpy as np
        N_NODES = 3125
        N_EDGES = 50000
        N_FEAT = 48
        N_EDGE_FEAT = 16
        HIDDEN = 128
        key = jax.random.key(seed)
        ks = jax.random.split(key, 8)
        tot = 2 * N_FEAT + N_EDGE_FEAT
        s1 = 1.0 / np.sqrt(tot)
        s2 = 1.0 / np.sqrt(HIDDEN)
        return {'x': jax.random.normal(ks[0], (N_NODES, N_FEAT), dtype=jnp.float32), 'edge_index': jax.random.randint(ks[1], (2, N_EDGES), 0, N_NODES, dtype=jnp.int64), 'edge_feat': jax.random.normal(ks[2], (N_EDGES, N_EDGE_FEAT), dtype=jnp.float32), 'W1': jax.random.normal(ks[3], (tot, HIDDEN), dtype=jnp.float32) * s1, 'b1': jnp.zeros((HIDDEN,), dtype=jnp.float32), 'W2': jax.random.normal(ks[4], (HIDDEN, HIDDEN), dtype=jnp.float32) * s2, 'b2': jnp.zeros((HIDDEN,), dtype=jnp.float32), 'W3': jax.random.normal(ks[5], (HIDDEN, N_FEAT), dtype=jnp.float32) * s2, 'b3': jnp.zeros((N_FEAT,), dtype=jnp.float32)}
    _L0_gnn_all = _L0_gnn_setup()
    _L0_gnn_in = {k: v for k, v in _L0_gnn_all.items() if k in ('W1', 'b1', 'W2', 'b2', 'W3', 'b3')}
    del _L0_gnn_all

    def _L1_gnn_setup():
        import jax, jax.numpy as jnp
        import numpy as np
        N_NODES = 50000
        N_EDGES = 50000
        IN_FEAT = 48
        OUT_FEAT = 48
        NUM_RELS = 8
        key = jax.random.key(seed)
        ks = jax.random.split(key, 9)
        s1 = float(np.sqrt(2.0) * np.sqrt(6.0 / (IN_FEAT + IN_FEAT)))
        s2 = float(np.sqrt(2.0) * np.sqrt(6.0 / (IN_FEAT + OUT_FEAT)))
        return {'inputs': jax.random.normal(ks[0], (N_NODES, IN_FEAT), dtype=jnp.float32), 'norm': jax.random.uniform(ks[1], (N_EDGES, 1), dtype=jnp.float32), 'weight1': jax.random.uniform(ks[2], (NUM_RELS, IN_FEAT, IN_FEAT), jnp.float32, -s1, s1), 'weight2': jax.random.uniform(ks[3], (NUM_RELS, IN_FEAT, OUT_FEAT), jnp.float32, -s2, s2), 'bias1': jax.random.normal(ks[4], (IN_FEAT,), dtype=jnp.float32) * 0.1, 'bias2': jax.random.normal(ks[5], (OUT_FEAT,), dtype=jnp.float32) * 0.1, 'src': jax.random.randint(ks[6], (N_EDGES,), 0, N_NODES, dtype=jnp.int64) if jax.config.jax_enable_x64 else jax.random.randint(ks[6], (N_EDGES,), 0, N_NODES).astype(jnp.int32), 'dst': jax.random.randint(ks[7], (N_EDGES,), 0, N_NODES).astype(jnp.int32), 'rel_type': jax.random.randint(ks[8], (N_EDGES,), 0, NUM_RELS).astype(jnp.int32)}
    _L1_gnn_all = _L1_gnn_setup()
    _L1_gnn_in = {k: v for k, v in _L1_gnn_all.items() if k in ('weight1', 'weight2', 'bias1', 'bias2')}
    del _L1_gnn_all

    def _L2_gnn_setup():
        import math
        import jax, jax.numpy as jnp
        import numpy as np
        N, E, C, T = (50000, 25000, 48, 128)
        C3, C9 = (C * 3, C * 9)
        EPS = 1e-05

        def sinusoidal_emb(t, dim):
            half = dim // 2
            freqs = jnp.exp(jnp.arange(half, dtype=jnp.float32) * (-math.log(10000.0) / (half - 1)))
            ang = t[:, None] * freqs[None, :]
            return jnp.concatenate([jnp.sin(ang), jnp.cos(ang)], axis=-1)

        def gcn_conv(x, W, b, src, dst, n):
            h = x @ W
            loop = jnp.arange(n, dtype=src.dtype)
            s = jnp.concatenate([src, loop])
            d = jnp.concatenate([dst, loop])
            deg = jax.ops.segment_sum(jnp.ones_like(d, dtype=h.dtype), d, num_segments=n)
            dinv = jnp.where(deg > 0, jax.lax.rsqrt(deg), 0.0)
            norm = dinv[s] * dinv[d]
            out = jax.ops.segment_sum(h[s] * norm[:, None], d, num_segments=n)
            return out + b

        def batchnorm(x, g, b):
            mean = jnp.mean(x, axis=0)
            var = jnp.mean(jnp.square(x - mean), axis=0)
            return g * (x - mean) * jax.lax.rsqrt(var + EPS) + b
        key = jax.random.key(seed)
        ks = jax.random.split(key, 12)
        rn = lambda k, sh: jax.random.normal(k, sh, jnp.float32) * 0.05
        return {'x': jax.random.normal(ks[0], (N, C), jnp.float32), 'edge_index': jax.random.randint(ks[1], (2, E), 0, N, dtype=jnp.int32), 'timestep': jax.random.randint(ks[2], (1,), 0, 1000).astype(jnp.float32), 'Wtm': rn(ks[3], (T, T)), 'btm': jnp.zeros((T,), jnp.float32), 'W_in': rn(ks[4], (C, C3)), 'b_in': jnp.zeros((C3,), jnp.float32), 'g_in': jnp.ones((C3,), jnp.float32), 'be_in': jnp.zeros((C3,), jnp.float32), 'Wt1': rn(ks[5], (T, C9)), 'bt1': jnp.zeros((C9,), jnp.float32), 'Wc1': rn(ks[6], (C3, C9)), 'bc1': jnp.zeros((C9,), jnp.float32), 'g1': jnp.ones((C9,), jnp.float32), 'be1': jnp.zeros((C9,), jnp.float32), 'Wt2': rn(ks[7], (T, C3)), 'bt2': jnp.zeros((C3,), jnp.float32), 'Wc2': rn(ks[8], (C9, C3)), 'bc2': jnp.zeros((C3,), jnp.float32), 'g2': jnp.ones((C3,), jnp.float32), 'be2': jnp.zeros((C3,), jnp.float32), 'W_out': rn(ks[9], (C3, C)), 'b_out': jnp.zeros((C,), jnp.float32), 'g_out': jnp.ones((C,), jnp.float32), 'be_out': jnp.zeros((C,), jnp.float32)}
    _L2_gnn_all = _L2_gnn_setup()
    _L2_gnn_in = {k: v for k, v in _L2_gnn_all.items() if k in ('timestep', 'Wtm', 'btm', 'W_in', 'b_in', 'g_in', 'be_in', 'Wt1', 'bt1', 'Wc1', 'bc1', 'g1', 'be1', 'Wt2', 'bt2', 'Wc2', 'bc2', 'g2', 'be2', 'W_out', 'b_out', 'g_out', 'be_out')}
    del _L2_gnn_all

    def _L3_gnn_setup():
        import jax, jax.numpy as jnp
        import numpy as np
        key = jax.random.key(seed)
        k1, k2 = jax.random.split(key)
        N, C, E = (3125, 48, 50000)
        label_mat = jax.random.uniform(k1, (N, C), dtype=jnp.float32)
        edge_index = jax.random.randint(k2, (2, E), 0, N, dtype=jnp.int64)
        return {'label_mat': label_mat, 'edge_index': edge_index, 'num_nodes': N}
    _L3_gnn_all = _L3_gnn_setup()
    _L3_gnn_in = {k: v for k, v in _L3_gnn_all.items() if k in ()}
    del _L3_gnn_all
    return {'x': x, 'src': src, 'dst': dst, 'edge_attr_16': edge_attr_16, 'edge_type_8': edge_type_8, 'edge_weight1': edge_weight1, 'L0_gnn_W1': _L0_gnn_in['W1'], 'L0_gnn_b1': _L0_gnn_in['b1'], 'L0_gnn_W2': _L0_gnn_in['W2'], 'L0_gnn_b2': _L0_gnn_in['b2'], 'L0_gnn_W3': _L0_gnn_in['W3'], 'L0_gnn_b3': _L0_gnn_in['b3'], 'L1_gnn_weight1': _L1_gnn_in['weight1'], 'L1_gnn_weight2': _L1_gnn_in['weight2'], 'L1_gnn_bias1': _L1_gnn_in['bias1'], 'L1_gnn_bias2': _L1_gnn_in['bias2'], 'L2_gnn_timestep': _L2_gnn_in['timestep'], 'L2_gnn_Wtm': _L2_gnn_in['Wtm'], 'L2_gnn_btm': _L2_gnn_in['btm'], 'L2_gnn_W_in': _L2_gnn_in['W_in'], 'L2_gnn_b_in': _L2_gnn_in['b_in'], 'L2_gnn_g_in': _L2_gnn_in['g_in'], 'L2_gnn_be_in': _L2_gnn_in['be_in'], 'L2_gnn_Wt1': _L2_gnn_in['Wt1'], 'L2_gnn_bt1': _L2_gnn_in['bt1'], 'L2_gnn_Wc1': _L2_gnn_in['Wc1'], 'L2_gnn_bc1': _L2_gnn_in['bc1'], 'L2_gnn_g1': _L2_gnn_in['g1'], 'L2_gnn_be1': _L2_gnn_in['be1'], 'L2_gnn_Wt2': _L2_gnn_in['Wt2'], 'L2_gnn_bt2': _L2_gnn_in['bt2'], 'L2_gnn_Wc2': _L2_gnn_in['Wc2'], 'L2_gnn_bc2': _L2_gnn_in['bc2'], 'L2_gnn_g2': _L2_gnn_in['g2'], 'L2_gnn_be2': _L2_gnn_in['be2'], 'L2_gnn_W_out': _L2_gnn_in['W_out'], 'L2_gnn_b_out': _L2_gnn_in['b_out'], 'L2_gnn_g_out': _L2_gnn_in['g_out'], 'L2_gnn_be_out': _L2_gnn_in['be_out']}

def reference(x, src, dst, edge_attr_16, edge_type_8, edge_weight1, L0_gnn_W1, L0_gnn_b1, L0_gnn_W2, L0_gnn_b2, L0_gnn_W3, L0_gnn_b3, L1_gnn_weight1, L1_gnn_weight2, L1_gnn_bias1, L1_gnn_bias2, L2_gnn_timestep, L2_gnn_Wtm, L2_gnn_btm, L2_gnn_W_in, L2_gnn_b_in, L2_gnn_g_in, L2_gnn_be_in, L2_gnn_Wt1, L2_gnn_bt1, L2_gnn_Wc1, L2_gnn_bc1, L2_gnn_g1, L2_gnn_be1, L2_gnn_Wt2, L2_gnn_bt2, L2_gnn_Wc2, L2_gnn_bc2, L2_gnn_g2, L2_gnn_be2, L2_gnn_W_out, L2_gnn_b_out, L2_gnn_g_out, L2_gnn_be_out):
    import jax
    import jax.numpy as jnp

    def _L0_gnn_ref(x, edge_index, edge_feat, W1, b1, W2, b2, W3, b3):
        import jax, jax.numpy as jnp
        import numpy as np
        N_NODES = 3125
        N_EDGES = 50000
        N_FEAT = 48
        N_EDGE_FEAT = 16
        HIDDEN = 128
        source = edge_index[0]
        target = edge_index[1]
        edge = jnp.concatenate([x[source], x[target], edge_feat], axis=-1)
        h = jax.nn.relu(edge @ W1 + b1)
        h = jax.nn.relu(h @ W2 + b2)
        message = h @ W3 + b3
        n = x.shape[0]
        msum = jax.ops.segment_sum(message, target, num_segments=n)
        cnt = jax.ops.segment_sum(jnp.ones((target.shape[0],), dtype=x.dtype), target, num_segments=n)
        update = msum / jnp.maximum(cnt, 1.0)[:, None]
        return x + update

    def _L1_gnn_ref(inputs, norm, weight1, weight2, bias1, bias2, src, dst, rel_type):
        import jax, jax.numpy as jnp
        import numpy as np
        N_NODES = 50000
        N_EDGES = 50000
        IN_FEAT = 48
        OUT_FEAT = 48
        NUM_RELS = 8
        h1 = jax.nn.relu(jnp.einsum('ni,rij->nrj', inputs, weight1) + bias1)
        h2 = jnp.einsum('nrj,rjo->nro', h1, weight2)
        msg = h2[src, rel_type] * norm
        agg = jax.ops.segment_sum(msg, dst, num_segments=inputs.shape[0])
        return jax.nn.relu(agg + bias2)

    def _L2_gnn_ref(x, edge_index, timestep, Wtm, btm, W_in, b_in, g_in, be_in, Wt1, bt1, Wc1, bc1, g1, be1, Wt2, bt2, Wc2, bc2, g2, be2, W_out, b_out, g_out, be_out):
        import math
        import jax, jax.numpy as jnp
        import numpy as np
        N, E, C, T = (50000, 25000, 48, 128)
        C3, C9 = (C * 3, C * 9)
        EPS = 1e-05

        def sinusoidal_emb(t, dim):
            half = dim // 2
            freqs = jnp.exp(jnp.arange(half, dtype=jnp.float32) * (-math.log(10000.0) / (half - 1)))
            ang = t[:, None] * freqs[None, :]
            return jnp.concatenate([jnp.sin(ang), jnp.cos(ang)], axis=-1)

        def gcn_conv(x, W, b, src, dst, n):
            h = x @ W
            loop = jnp.arange(n, dtype=src.dtype)
            s = jnp.concatenate([src, loop])
            d = jnp.concatenate([dst, loop])
            deg = jax.ops.segment_sum(jnp.ones_like(d, dtype=h.dtype), d, num_segments=n)
            dinv = jnp.where(deg > 0, jax.lax.rsqrt(deg), 0.0)
            norm = dinv[s] * dinv[d]
            out = jax.ops.segment_sum(h[s] * norm[:, None], d, num_segments=n)
            return out + b

        def batchnorm(x, g, b):
            mean = jnp.mean(x, axis=0)
            var = jnp.mean(jnp.square(x - mean), axis=0)
            return g * (x - mean) * jax.lax.rsqrt(var + EPS) + b
        src, dst = (edge_index[0], edge_index[1])
        n = x.shape[0]
        relu = jax.nn.relu
        t = relu(sinusoidal_emb(timestep, T) @ Wtm + btm)
        h = relu(batchnorm(gcn_conv(x, W_in, b_in, src, dst, n), g_in, be_in))
        te1 = relu(t @ Wt1 + bt1)
        h = batchnorm(relu(gcn_conv(h, Wc1, bc1, src, dst, n) + te1), g1, be1)
        te2 = relu(t @ Wt2 + bt2)
        h = batchnorm(relu(gcn_conv(h, Wc2, bc2, src, dst, n) + te2), g2, be2)
        return relu(batchnorm(gcn_conv(h, W_out, b_out, src, dst, n), g_out, be_out))

    def _L3_gnn_ref(label_mat, edge_index, num_nodes):
        import jax, jax.numpy as jnp
        import numpy as np
        row, col = (edge_index[0], edge_index[1])
        self_loop = jnp.arange(num_nodes, dtype=row.dtype)
        row = jnp.concatenate([row, self_loop])
        col = jnp.concatenate([col, self_loop])
        ones = jnp.ones_like(row, dtype=label_mat.dtype)
        deg = jax.ops.segment_sum(ones, row, num_segments=num_nodes)
        deg_inv_sqrt = jnp.where(deg > 0, jax.lax.rsqrt(deg), 0.0)
        norm = deg_inv_sqrt[row] * deg_inv_sqrt[col]
        msgs = label_mat[row] * norm[:, None]
        out = jax.ops.segment_sum(msgs, col, num_segments=num_nodes)
        return out
    edge_index = jnp.stack([src, dst])
    x = _layernorm(x + _L0_gnn_ref(x, edge_index, edge_attr_16, L0_gnn_W1, L0_gnn_b1, L0_gnn_W2, L0_gnn_b2, L0_gnn_W3, L0_gnn_b3), axis=-1)
    x = _layernorm(x + _L1_gnn_ref(x, edge_weight1, L1_gnn_weight1, L1_gnn_weight2, L1_gnn_bias1, L1_gnn_bias2, src, dst, edge_type_8), axis=-1)
    x = _layernorm(x + _L2_gnn_ref(x, edge_index, L2_gnn_timestep, L2_gnn_Wtm, L2_gnn_btm, L2_gnn_W_in, L2_gnn_b_in, L2_gnn_g_in, L2_gnn_be_in, L2_gnn_Wt1, L2_gnn_bt1, L2_gnn_Wc1, L2_gnn_bc1, L2_gnn_g1, L2_gnn_be1, L2_gnn_Wt2, L2_gnn_bt2, L2_gnn_Wc2, L2_gnn_bc2, L2_gnn_g2, L2_gnn_be2, L2_gnn_W_out, L2_gnn_b_out, L2_gnn_g_out, L2_gnn_be_out), axis=-1)
    x = _layernorm(x + _L3_gnn_ref(x, edge_index, 3125), axis=-1)
    return x

_drawn_inputs = setup_inputs


def setup_inputs(seed=0):
    import zlib

    import numpy as np

    out = dict(_drawn_inputs(seed))
    spreads = {'L0_gnn_b1': (0.0, 0.308),
     'L0_gnn_b2': (0.0, 0.1),
     'L0_gnn_b3': (0.0, 0.1),
     'L2_gnn_btm': (0.0, 0.1),
     'L2_gnn_b_in': (0.0, 0.8),
     'L2_gnn_g_in': (1.0, 0.2),
     'L2_gnn_be_in': (0.0, 0.1),
     'L2_gnn_bt1': (0.0, 0.1),
     'L2_gnn_bc1': (0.0, 0.1),
     'L2_gnn_g1': (1.0, 0.2),
     'L2_gnn_be1': (0.0, 0.1),
     'L2_gnn_bt2': (0.0, 0.1),
     'L2_gnn_bc2': (0.0, 0.1),
     'L2_gnn_g2': (1.0, 0.2),
     'L2_gnn_be2': (0.0, 0.627),
     'L2_gnn_b_out': (0.0, 0.8),
     'L2_gnn_g_out': (1.0, 0.2),
     'L2_gnn_be_out': (0.0, 0.1)}
    factors = {'edge_attr_16': 3.711}
    for name, (base, spread) in spreads.items():
        noise = np.random.default_rng([zlib.crc32(name.encode()), seed]).standard_normal(out[name].shape)
        drawn = base * np.exp(spread * noise) if base else spread * noise
        out[name] = jnp.asarray(drawn.astype(out[name].dtype))
    for name, factor in factors.items():
        out[name] = (out[name] * factor).astype(out[name].dtype)
    return out
```

```python
from contextlib import ExitStack

import numpy as np

import concourse.bass as bass
from concourse import mybir

F32 = mybir.dt.float32
I32 = mybir.dt.int32
BF16 = mybir.dt.bfloat16
ALU = mybir.AluOpType
ACT = mybir.ActivationFunctionType
AX = mybir.AxisListType

N = 3125
E = 103125
TN = 125
NT = N // TN
CE = 128
NC = -(-E // CE)
PADDED_DST = 100000
STEPS = 832
G = 4
NG = STEPS // G
RING = 4
SB = -(-STEPS // CE)
F = 48
H = 128
C3 = 3 * F
C9 = 9 * F
NR = 8
HALF = C3 // 2
QUART = C9 // 4
BT = 5
NB = NT // BT
BN = BT * TN
EPS = 1e-5
ROUND = 12582912.0

PASSES = [(F, True), (F, False), (C3, False), (C3, False), (F, False), (F, False)]


def build(nc, a, out):
    with ExitStack() as ctx:
        def sb(name, shape, dt=F32):
            return ctx.enter_context(nc.sbuf_tensor(name, shape, dt))

        def sem(name):
            return ctx.enter_context(nc.semaphore(name))

        def dram(name, shape, dt=F32):
            return nc.dram_tensor(name, shape, dt, kind="Internal").ap()

        src_hidden = dram("src_hidden", (N, H))
        rel_table = dram("rel_table", (N * NR, F))
        conv_table = dram("conv_table", (N, C3))
        conv_table48 = dram("conv_table48", (N, F))
        step_row = dram("step_row", (2, SB * CE), I32)

        src_idx = sb("src_idx", [CE, SB * CE], I32)
        rel_idx = sb("rel_idx", [CE, SB * CE], I32)
        dst_rel = sb("dst_rel", [CE, SB * CE])
        wgt = sb("wgt", [CE, SB * CE])
        step_regs = sb("step_regs", [1, 2, SB * CE], I32)
        iota_i = sb("iota_i", [CE, CE], I32)
        iota = sb("iota", [CE, CE])
        part_i = sb("part_i", [CE, SB], I32)
        step_no = sb("step_no", [CE, SB])
        ident = sb("ident", [CE, CE])
        ones_row = sb("ones_row", [1, CE])
        w1ab = sb("w1ab", [F, 2, H])
        w1c = sb("w1c", [16, H])
        b1 = sb("b1", [TN, H])
        w2 = sb("w2", [H, H])
        b2 = sb("b2", [1, H])
        w3 = sb("w3", [H, F])
        b3 = sb("b3", [TN, F])
        rel_w1 = sb("rel_w1", [F, NR, F])
        rel_w2 = sb("rel_w2", [2 * F, 4, 2 * F])
        rel_b1 = sb("rel_b1", [2 * F, 1])
        rel_b2 = sb("rel_b2", [TN, F])
        w_in = sb("w_in", [F, C3])
        wc1 = sb("wc1", [HALF, 2, C9])
        wc2 = sb("wc2", [QUART, 4, C3])
        w_out = sb("w_out", [HALF, 2, F])
        wtm = sb("wtm", [H, H])
        wt1 = sb("wt1", [H, C9])
        wt2 = sb("wt2", [H, C3])
        col_in = sb("col_in", [HALF, 3, 2])
        col_1 = sb("col_1", [QUART, 4, 4])
        col_2 = sb("col_2", [HALF, 4, 2])
        col_out = sb("col_out", [F, 3, 1])
        time_col = sb("time_col", [H, 12])
        x0 = sb("x0", [TN, NT, F])
        x_cur = sb("x_cur", [TN, NT, F])
        y = sb("y", [TN, NT, F])
        scratch = sb("scratch", [TN, NT, F])
        acc = sb("acc", [TN, NT, C3])
        table = sb("table", [CE, NT, C3])
        deg = sb("deg", [TN, 8, NT])
        red = sb("red", [TN, 6, NT])
        feat = sb("feat", [CE, 4, N])
        stats = sb("stats", [CE, 4, NB, 2, 6])
        bn = sb("bn", [CE, 4, 8])
        rows = sb("rows", [CE, RING, G, C3])
        hot = sb("hot", [CE, RING, G, TN])
        idx = sb("idx", [CE, RING, G], I32)
        z = sb("z", [CE, 4 * BN])
        zt = sb("zt", [CE, 2 * BN])
        psum = ctx.enter_context(nc.psum_tensor("psum", [CE, 8, 512], F32))

        flat = feat[:, :, :].rearrange("p a n -> p (a n)")
        at = [0]

        def carve(parts, *dims):
            size = int(np.prod(dims))
            v = flat[0:parts, at[0]:at[0] + size]
            at[0] += size
            names = "abcd"[:len(dims)]
            return v.rearrange(f"p ({' '.join(names)}) -> p {' '.join(names)}",
                               **dict(zip(names, dims))) if len(dims) > 1 else v

        start_bc = carve(CE, NC)
        jump_bc = carve(CE, NC)
        mask = carve(CE, NC)
        first = carve(1, NC)
        last = carve(1, NC)
        run = carve(1, 2, NC)
        ends = carve(1, 2, NC).bitcast(I32)
        step_e = carve(CE, 2, 4, CE).bitcast(I32)
        step_f = carve(CE, 6, CE)
        cols = carve(CE, 6, SB)
        cols_i = carve(CE, 2, SB).bitcast(I32)
        assert at[0] <= 4 * N
        at[0] = 0
        dst_half_sb = carve(TN, NT, H)
        attr = carve(16, RING, G * CE)
        hot_t = carve(TN, G, CE)
        pre = carve(CE, G, H)
        h1 = carve(H, G * CE)
        h2 = carve(CE, G, H + 1)
        xt = carve(F, BT, TN)
        src_half_sb = carve(TN, BT, H)
        assert at[0] <= 4 * N
        at[0] = 0
        rel_h = carve(2 * F, 4, BN)
        rel_out = carve(TN, BT, NR * F)
        src_lo = table[:, 0:12, :].rearrange("p a b -> p (a b)")[:, 0:SB * CE]
        src_hi = table[:, 12:24, :].rearrange("p a b -> p (a b)")[:, 0:SB * CE]
        lo_hot = carve(CE, 2, G, TN)
        hi_hot = carve(CE, 2, G, NT)
        assert at[0] <= 4 * N

        CNT, RCNT, BSCALE, DINV, ODINV, T0, T1 = range(7)

        weights_in = sem("weights_in")
        vec_step = sem("vec_step")
        ends_in = sem("ends_in")

        step_in = [sem(f"step_in_{k}") for k in range(2)]
        rows_bc = sem("rows_bc")
        rows_in = sem("rows_in")
        start_copied = sem("start_copied")
        iota_made = sem("iota_made")
        turn_rows = sem("turn_rows")
        turned_rows = sem("turned_rows")
        step_idx = sem("step_idx")
        regs_out = sem("regs_out")
        regs_in = sem("regs_in")
        tables_made = sem("tables_made")
        consts_made = sem("consts_made")
        xt_in = sem("xt_in")
        node_prod = sem("node_prod")
        src_half = sem("src_half")
        dst_half = sem("dst_half")
        src_half_out = sem("src_half_out")
        attr_in = [sem(f"attr_in_{k}") for k in range(RING)]
        gathered = [sem(f"gathered_{k}") for k in range(RING)]
        idx_ready = sem("idx_ready")
        hot_ready = sem("hot_ready")
        hot_turned = sem("hot_turned")
        hot_t_ready = sem("hot_t_ready")
        edge_sum = sem("edge_sum")
        edge_pre = sem("edge_pre")
        pre_turned = sem("pre_turned")
        h1_ready = sem("h1_ready")
        h2_made = sem("h2_made")
        h2_ready = sem("h2_ready")
        spread = sem("spread")
        added = sem("added")
        p_idx = sem("p_idx")
        p_hot = sem("p_hot")
        p_sum = sem("p_sum")
        p_added = sem("p_added")
        histogram = sem("histogram")
        prepared = sem("prepared")
        turned = sem("turned")
        turned_in = sem("turned_in")
        product = sem("product")
        stored = sem("stored")
        product2 = sem("product2")
        stored2 = sem("stored2")
        stats_made = sem("stats_made")
        table_ready = sem("table_ready")
        table_out = sem("table_out")
        var_ready = sem("var_ready")
        std_ready = sem("std_ready")
        affine = sem("affine")
        time_r = sem("time_r")
        time_emb = sem("time_emb")
        time_prod = sem("time_prod")
        time_act = sem("time_act")
        acc_clear = sem("acc_clear")
        result = sem("result")
        result_out = sem("result_out")


        USERS = {"prepared": range(10), "turned": [0, 1, 2, 3, 4, 6, 8, 9], "turned_in": [0, 1, 2, 4],
                 "product": [0, 1, 2, 4, 5, 7], "stored": range(10), "stats": [2, 4, 6, 8]}

        def counted(name, k):
            return 1 + NB * sum(u < k for u in USERS[name])

        def rows_of(i, n=BT):
            return bass.ds(i * n, n)

        def bcast(ap, n, f):
            return ap.unsqueeze(2).to_broadcast([ap.shape[0], n, f])

        def slots(bank, n, width=TN, parts=CE):
            v = psum[0:parts, bank:8, :].rearrange("p b c -> p (b c)")
            return v[:, 0:128 * n].rearrange("p (s c) -> p s c", c=128)[:, :, 0:width]

        def wide(bank, n, width, parts=TN, stride=256):
            v = psum[0:parts, bank:8, :].rearrange("p b c -> p (b c)")
            return v[:, 0:stride * n].rearrange("p (s c) -> p s c", c=stride)[:, :, 0:width]

        ctx.enter_context(nc.allow_non_contiguous_dma(reason="a few hundred words, once"))
        block = ctx.enter_context(nc.Block())

        @block.sync
        def _(sp):
            sp.dma_start(ends[:, 0, :], a["dst"][:, 0:1].rearrange("c k -> k c")).then_inc(ends_in, 16)
            sp.dma_start(ends[:, 1, 0:NC - 1],
                         a["dst"][0:NC - 1, CE - 1:CE].rearrange("c k -> k c")).then_inc(ends_in, 16)
            tail = E - 1 - (NC - 1) * CE
            sp.dma_start(ends[:, 1, NC - 1:NC], a["dst"][NC - 1:NC, tail:tail + 1]).then_inc(ends_in, 16)
            loads = [
                (x0[:, :, :], a["x"].rearrange("(t p) f -> p t f", p=TN)),
                (w1ab[:, :, :], a["W1"][0:2 * F, :].rearrange("(s k) h -> k s h", s=2)),
                (w1c[:, :], a["W1"][2 * F:2 * F + 16, :]),
                (b1[:, :], a["b1"].partition_broadcast(TN)),
                (w2[:, :], a["W2"]),
                (b2[:, :], a["b2"].unsqueeze(0)),
                (w3[:, :], a["W3"]),
                (b3[:, :], a["b3"].partition_broadcast(TN)),
                (rel_w1[:, :, :], a["rw1"].rearrange("r i j -> i r j")),
                (rel_b1[0:F, :], a["rb1"].unsqueeze(1)),
                (rel_b1[F:2 * F, :], a["rb1"].unsqueeze(1)),
                (rel_b2[:, :], a["rb2"].partition_broadcast(TN)),
                (w_in[:, :], a["W_in"]),
                (wc1[:, :, :], a["Wc1"].rearrange("(s k) h -> k s h", s=2)),
                (wc2[:, :, :], a["Wc2"].rearrange("(s k) h -> k s h", s=4)),
                (w_out[:, :, :], a["W_out"].rearrange("(s k) h -> k s h", s=2)),
                (wtm[:, :], a["Wtm"]),
                (wt1[:, :], a["Wt1"]),
                (wt2[:, :], a["Wt2"]),
                (time_col[:, 0:2], a["time_const"]),
                (time_col[:, 2:3], a["timestep"].partition_broadcast(H)),
                (time_col[:, 3:4], a["btm"].unsqueeze(1)),
            ]
            for dst_, names, n in ((col_in, ("b_in", "g_in", "be_in"), 2), (col_1, ("bc1", "g1", "be1", "bt1"), 4),
                                   (col_2, ("bc2", "g2", "be2", "bt2"), 2), (col_out, ("b_out", "g_out", "be_out"), 1)):
                for r, name in enumerate(names):
                    loads.append((dst_[:, r, :], a[name].rearrange("(s k) -> k s", s=n)))
            for q in range(4):
                loads.append((rel_w2[0:F, q, 0:F], a["rw2"][2 * q]))
                loads.append((rel_w2[F:2 * F, q, F:2 * F], a["rw2"][2 * q + 1]))
            sp.wait_ge(consts_made, 1)
            for to, frm in loads:
                sp.dma_start(to, frm).then_inc(weights_in, 16)
            assert len(loads) == N_LOADS, len(loads)

            sp.wait_ge(step_idx, 1)
            for r in range(2):
                sp.dma_start(step_row[r].rearrange("(j p) -> p j", p=CE), cols_i[:, r, :]).then_inc(regs_out, 16)
            sp.wait_ge(regs_out, 32)
            sp.dma_start(step_regs[:, :, :], step_row.unsqueeze(0)).then_inc(regs_in, 16)

            sp.wait_ge(tables_made, SB)
            for i in range(NB):
                if i:
                    sp.wait_ge(src_half, i)
                sp.dma_start(xt[:, :, :], a["xT"][:, i * BN:(i + 1) * BN].rearrange("f (u p) -> f u p", p=TN)
                             ).then_inc(xt_in, 16)
                sp.wait_ge(src_half, i + 1)
                sp.dma_start(src_hidden[i * BN:(i + 1) * BN, :].rearrange("(u p) h -> p u h", p=TN),
                             src_half_sb[:, :, :]).then_inc(src_half_out, 16)

            sp.wait_ge(regs_in, 16)

            def load_attr(g, u):
                _, chunk = nc.values_load_multi_w_load_instructions(
                    step_regs[0:1, 1, bass.ds(g * G, G)], engines=[sp.engine], min_val=0, max_val=NC - 1,
                    skip_runtime_bounds_check_because="the table holds chunk numbers")
                for k in range(G):
                    sp.dma_start(attr[:, u, k * CE:(k + 1) * CE],
                                 a["attrT"][:, bass.ds(chunk[k] * CE, CE)]).then_inc(attr_in[u], 16)

            for g in range(RING):
                load_attr(g, g)
            with sp.Fori(1, NG // RING) as i:
                for u in range(RING):
                    sp.wait_ge(edge_sum, (i - 1) * RING + u + 1)
                    load_attr(i * RING + u, u)

            for i in range(NB):
                sp.wait_ge(stored2, i + 2)
                sp.dma_start(rel_table.rearrange("(b u p r) f -> b p u (r f)", u=BT, p=TN, r=NR)[i],
                             rel_out[:, :, :]).then_inc(table_out, 16)
            for k, (width, _w) in enumerate(PASSES[1:]):
                sp.wait_ge(table_ready, k + 1)
                dst_ = conv_table if width == C3 else conv_table48
                sp.dma_start(dst_.rearrange("(t p) f -> p t f", p=TN), table[0:TN, :, 0:width]).then_inc(table_out, 16)
            sp.wait_ge(result, 1)
            sp.dma_start(out.rearrange("(t p) f -> p t f", p=TN), y[:, :, :]).then_inc(result_out, 16)
            sp.wait_ge(result_out, 16)

        @block.gpsimd
        def _(pool):
            nc.gpsimd.iota(iota_i[:, :], [[1, CE]], base=0, channel_multiplier=0).then_inc(iota_made, 1)
            nc.gpsimd.iota(part_i[:, :], [[CE, SB]], base=0, channel_multiplier=1).then_inc(iota_made, 1)
            nc.gpsimd.memset(ident[:, :], 0.0).then_inc(iota_made, 1)
            pool.wait_ge(iota_made, 3)
            nc.gpsimd.affine_select(out=ident[:, :], in_=ident[:, :], compare_op=ALU.not_equal, fill=1.0,
                                    base=0, pattern=[[-1, CE]], channel_multiplier=1).then_inc(iota_made, 1)

            pool.wait_ge(step_idx, 1)
            for j in range(SB):
                if j >= 2:
                    pool.wait_ge(turn_rows, j - 1)
                pool.nop(nofuse=True)
                for r, name in enumerate(("dst", "src", "type", "w")):
                    to = step_e[:, j % 2, r, :]
                    pool.indirect_dma_start(to if name != "w" else to.bitcast(F32), None, a[name],
                                            bass.IndirectOffsetOnAxis(ap=cols_i[:, 1, j:j + 1], axis=0)
                                            ).then_inc(step_in[j % 2], 16)

            def gather(tab, width, u):
                for k in range(G):
                    pool.indirect_dma_start(rows[:, u, k, 0:width], None, tab,
                                            bass.IndirectOffsetOnAxis(ap=idx[:, u, k:k + 1], axis=0)
                                            ).then_inc(gathered[u], 16)

            def pass_gathers(tab, width, ready, base):
                for g in range(RING):
                    pool.wait_ge(ready, base + g + 1)
                    pool.nop(nofuse=True)
                    gather(tab, width, g)
                with pool.Fori(1, NG // RING) as i:
                    for u in range(RING):
                        pool.wait_ge(ready, i * RING + (base + u + 1))
                        pool.nop(nofuse=True)
                        gather(tab, width, u)

            pool.wait_ge(src_half_out, 16 * NB)
            pass_gathers(src_hidden, H, idx_ready, 0)
            for k, (width, weighted) in enumerate(PASSES):
                pool.wait_ge(table_out, 16 * (NB + k))
                tab = rel_table if weighted else conv_table if width == C3 else conv_table48
                pass_gathers(tab, width, p_idx, NG * k)

        @block.tensor
        def _(pe):
            pe.sem_inc(turned, 1)
            pe.sem_inc(product, 1)
            pe.sem_inc(product2, 1)
            pe.sem_inc(p_sum, 1)
            pe.sem_inc(spread, 1)
            pe.wait_ge(rows_bc, 1)
            half = NC // 2
            for b in range(4):
                mm = pe.matmul(psum[:, b, 0:half], ones_row[:, :], run[:, b // 2, (b % 2) * half:(b % 2 + 1) * half],
                               start=True, stop=True)
            mm.then_inc(rows_in, 1)
            pe.wait_ge(iota_made, 4)
            for j in range(SB):
                pe.wait_ge(turn_rows, j + 1)
                if j:
                    pe.wait_ge(tables_made, j)
                else:
                    pe.wait_ge(start_copied, 1)
                for r in range(6):
                    tr = pe.transpose(psum[:, r // 4, (r % 4) * CE:(r % 4 + 1) * CE], step_f[:, r, :], ident[:, :])
                tr.then_inc(turned_rows, 1)
            pe.wait_ge(weights_in, 16 * N_LOADS)
            for i in range(NB):
                pe.wait_ge(xt_in, 16 * (i + 1))
                if i:
                    pe.wait_ge(src_half, i)
                    pe.wait_ge(dst_half, i)
                for u in range(BT):
                    mm = pe.matmul(psum[0:TN, u, 0:2 * H], xt[:, u, :],
                                   w1ab[:, :, :].rearrange("k s h -> k (s h)"), start=True, stop=True)
                mm.then_inc(node_prod, 1)

            pe.wait_ge(time_r, 1)
            pe.matmul(psum[:, 7, 0:1], wtm[:, :], time_col[:, 4:5], start=True, stop=True).then_inc(time_prod, 1)
            pe.wait_ge(time_act, 1)
            for m in range(4):
                pe.matmul(psum[0:QUART, 7, 1 + m:2 + m], wt1[:, m * QUART:(m + 1) * QUART], time_col[:, 5:6],
                          start=True, stop=True)
            for m in range(2):
                mm = pe.matmul(psum[0:HALF, 7, 5 + m:6 + m], wt2[:, m * HALF:(m + 1) * HALF], time_col[:, 5:6],
                               start=True, stop=True)
            mm.then_inc(time_prod, 1)
            pe.wait_ge(time_act, 2)

            def turn_hot(g, u):
                pe.wait_ge(hot_ready, g + 1)
                for k in range(G):
                    tr = pe.transpose(psum[0:TN, 0, k * CE:(k + 1) * CE], hot[:, u, k, :], ident[:, :])
                tr.then_inc(hot_turned, 1)

            def sum_edge(g, u, n):
                _, tile = nc.values_load_multi_w_load_instructions(
                    step_regs[0:1, 0, bass.ds(g * G, G)], engines=[pe.engine], min_val=0, max_val=NT - 1,
                    skip_runtime_bounds_check_because="the table is clamped to the tiles")
                pe.wait_ge(hot_t_ready, g + 1)
                pe.wait_ge(attr_in[u], n)
                for k in range(G):
                    o = psum[:, 1, k * H:(k + 1) * H]
                    pe.matmul(o, attr[:, u, k * CE:(k + 1) * CE], w1c[:, :], start=True, stop=False)
                    mm = pe.matmul(o, hot_t[:, k, :],
                                   dst_half_sb[:, bass.ds(tile[k], 1), :].rearrange("p a h -> p (a h)"),
                                   start=False, stop=True)
                mm.then_inc(edge_sum, 1)

            def turn_pre(g):
                pe.wait_ge(edge_pre, g + 1)
                for k in range(G):
                    tr = pe.transpose(psum[:, 2, k * CE:(k + 1) * CE], pre[:, k, :], ident[:, :])
                tr.then_inc(pre_turned, 1)

            def make_h2(g):
                pe.wait_ge(h1_ready, g + 1)
                for k in range(G):
                    o = psum[:, 3, k * H:(k + 1) * H]
                    pe.matmul(o, h1[:, k * CE:(k + 1) * CE], w2[:, :], start=True, stop=False)
                    mm = pe.matmul(o, ones_row[:, :], b2[:, :], start=False, stop=True)
                mm.then_inc(h2_made, 1)

            def spread_out(g, u):
                pe.wait_ge(h2_ready, g + 1)
                pe.wait_ge(added, g * G - G + 1 if not isinstance(g, int) else max(g * G - G, 0) + 1)
                par = u % 2
                for k in range(G):
                    c = (k % 2) * (H + 1)
                    mm = pe.matmul(psum[0:TN, 4 + 2 * par + k // 2, c:c + H + 1], hot[:, u, k, :], h2[:, k, :],
                                   start=True, stop=True)
                mm.then_inc(spread, 1)

            def edge_slot(g, u, n):
                if not isinstance(g, int) or g < NG:
                    turn_hot(g, u)
                if not isinstance(g, int) or 1 <= g < NG + 1:
                    turn_pre(g - 1)
                if not isinstance(g, int) or 2 <= g:
                    spread_out(g - 2, (u - 2) % RING)
                if not isinstance(g, int) or g < NG:
                    sum_edge(g, u, n)
                if not isinstance(g, int) or 1 <= g < NG + 1:
                    make_h2(g - 1)

            for g in range(RING):
                edge_slot(g, g, 16 * G)
            with pe.Fori(1, NG // RING) as i:
                for u in range(RING):
                    edge_slot(i * RING + u, u, (i + 1) * (16 * G))
            for g in range(NG, NG + 2):
                edge_slot(g, g % RING, 0)

            def per_block(body):
                with pe.Fori(0, NB) as i:
                    body(i)

            def turn(k, i, width, after):
                pe.wait_ge(prepared, i + counted("prepared", k) + 1)
                pe.wait_ge(after, i + counted({turned_in: "turned_in", stored: "stored"}[after], k))
                pe.nop(nofuse=True)
                halves = 1 if width in (F, H) else 2
                w = width // halves
                zz = z[0:TN, 0:BT * width].rearrange("p (u s f) -> p u s f", u=BT, s=halves)
                for s in range(halves):
                    for u in range(BT):
                        tr = pe.transpose(slots(0, 10, TN, w)[:, s * BT + u, :], zz[:, u, s, :], ident[0:TN, 0:TN])
                tr.then_inc(turned, 1)

            def by_bank(first_slot):
                n = min(BT, 4 - first_slot % 4)
                return [(0, n), (n, BT - n)]

            def feature_product(w, mo, first, k_parts, ins):
                for a0, n in by_bank(mo * BT):
                    for ki, (wk, zk) in enumerate(zip(w, ins)):
                        mm = pe.matmul(slots(3, 20, TN, first)[:, mo * BT + a0:mo * BT + a0 + n, :], wk,
                                       zk[:, a0 * TN:(a0 + n) * TN].rearrange("p (s c) -> p s c", c=TN),
                                       start=(ki == 0), stop=(ki == len(w) - 1))
                return mm

            def st0(i):
                turn(0, i, H, turned_in)
                pe.wait_ge(turned_in, i + counted("turned_in", 0) + 1)
                pe.wait_ge(stored, i + counted("stored", 0))
                for u in range(BT):
                    mm = pe.matmul(psum[0:TN, 3, u * F:(u + 1) * F], zt[:, u * TN:(u + 1) * TN], w3[:, :],
                                   start=True, stop=True)
                mm.then_inc(product, 1)

            def st1(i):
                turn(1, i, F, turned_in)
                pe.wait_ge(turned_in, i + counted("turned_in", 1) + 1)
                pe.wait_ge(stored2, i + 1)
                for q in range(4):
                    mm = feature_product([rel_w1[:, 2 * q:2 * q + 2, :].rearrange("k r j -> k (r j)")], q, 2 * F, 1,
                                         [zt[0:F, 0:BN]])
                mm.then_inc(product, 1)
                pe.wait_ge(stored, i + counted("stored", 1) + 1)
                for u in range(BT):
                    for q in range(4):
                        mm = pe.matmul(psum[0:TN, 3 + u, q * 2 * F:(q + 1) * 2 * F],
                                       rel_h[:, q, u * TN:(u + 1) * TN], rel_w2[:, q, :], start=True, stop=True)
                mm.then_inc(product2, 1)

            def st2(i):
                turn(2, i, F, turned_in)
                pe.wait_ge(turned_in, i + counted("turned_in", 2) + 1)
                pe.wait_ge(stored, i + counted("stored", 2))
                for m in range(2):
                    mm = feature_product([w_in[:, m * HALF:(m + 1) * HALF]], m, HALF, 1, [zt[0:F, 0:BN]])
                mm.then_inc(product, 1)

            def turn_back(k, i, parts, halves):
                pe.wait_ge(prepared, i + counted("prepared", k) + 1)
                pe.wait_ge(stored, i + counted("stored", k))
                pe.nop(nofuse=True)
                for u in range(BT):
                    for s in range(halves):
                        tr = pe.transpose(wide(0, BT, C3)[:, u, s * parts:(s + 1) * parts],
                                          z[0:parts, s * BN + u * TN:s * BN + (u + 1) * TN], ident[0:parts, 0:parts])
                tr.then_inc(turned, 1)

            def st4(i):
                turn(4, i, C3, turned_in)
                pe.wait_ge(turned_in, i + counted("turned_in", 4) + 1)
                pe.wait_ge(stored, i + counted("stored", 4))
                for m in range(4):
                    mm = feature_product([wc1[:, s, m * QUART:(m + 1) * QUART] for s in range(2)], m, QUART, 2,
                                         [zt[0:HALF, s * BN:(s + 1) * BN] for s in range(2)])
                mm.then_inc(product, 1)

            def node_product(k, i, parts, n, w, width):
                pe.wait_ge(prepared, i + counted("prepared", k) + 1)
                pe.wait_ge(stored, i + counted("stored", k))
                for u in range(BT):
                    for s in range(n):
                        mm = pe.matmul(wide(0, BT, width)[:, u, :], z[0:parts, s * BN + u * TN:s * BN + (u + 1) * TN],
                                       w[:, s, :], start=(s == 0), stop=(s == n - 1))
                mm.then_inc(product, 1)

            def pass_sums(k, width, weighted):
                def slot(g, u, n):
                    first_ = isinstance(g, int) and g == 0
                    pe.wait_ge(p_hot, g + (NG * k + 1))
                    pe.wait_ge(p_added, (g - 2) * G + (G * NG * k + G + 1) if not isinstance(g, int)
                               else G * NG * k + G * max(g - 1, 0) + 1)
                    pe.wait_ge(gathered[u], n)
                    for s in range(G):
                        c = (s % 2) * C3
                        mm = pe.matmul(psum[0:TN, 2 * (u % 2) + s // 2, c:c + width], hot[:, u, s, :],
                                       rows[:, u, s, 0:width], start=True, stop=True)
                        if weighted:
                            mm = pe.matmul(psum[0:TN, 6, 0:NT], lo_hot[:, u % 2, s, :], hi_hot[:, u % 2, s, :],
                                           start=(first_ and s == 0), stop=False, skip_group_check=True)
                    mm.then_inc(p_sum, 1)

                n0 = 16 * G * (NG // RING) * (k + 1)
                for g in range(RING):
                    slot(g, g, n0 + 16 * G)
                with pe.Fori(1, NG // RING) as i:
                    for u in range(RING):
                        slot(i * RING + u, u, i * (16 * G) + (n0 + 16 * G))

            per_block(st0)
            per_block(st1)
            pass_sums(0, *PASSES[0])
            pass_sums(1, *PASSES[1])
            per_block(st2)
            per_block(lambda i: turn_back(3, i, HALF, 2))
            pass_sums(2, *PASSES[2])
            per_block(st4)
            per_block(lambda i: node_product(5, i, QUART, 4, wc2, C3))
            pass_sums(3, *PASSES[3])
            per_block(lambda i: turn(6, i, C3, stored))
            per_block(lambda i: node_product(7, i, HALF, 2, w_out, F))
            pass_sums(4, *PASSES[4])
            per_block(lambda i: turn(8, i, F, stored))
            per_block(lambda i: turn_back(9, i, F, 1))
            pass_sums(5, *PASSES[5])

        @block.scalar
        def _(act):
            act.sem_inc(turned_in, 1)
            A = nc.scalar.activation

            for i in range(NB):
                act.wait_ge(node_prod, i + 1)
                if i:
                    act.wait_ge(src_half_out, 16 * i)
                A(src_half_sb[:, :, :], psum[0:TN, 0:BT, 0:H], ACT.Copy).then_inc(src_half, 1)

            act.wait_ge(time_emb, 1)
            A(time_col[:, 4:5], time_col[:, 6:7], ACT.Sin).then_inc(time_r, 1)
            act.wait_ge(time_prod, 1)
            A(time_col[:, 5:6], psum[:, 7, 0:1], ACT.Relu, bias=time_col[:, 3:4]).then_inc(time_act, 1)
            act.wait_ge(time_prod, 2)
            for m in range(4):
                A(bn[0:QUART, m, 7:8], psum[0:QUART, 7, 1 + m:2 + m], ACT.Relu, bias=col_1[:, 3, m:m + 1])
            for m in range(2):
                last_ = A(bn[0:HALF, m, 6:7], psum[0:HALF, 7, 5 + m:6 + m], ACT.Relu, bias=col_2[:, 3, m:m + 1])
            last_.then_inc(time_act, 1)

            def copy_hot_t(g):
                act.wait_ge(hot_turned, g + 1)
                A(hot_t[:, :, :], psum[0:TN, 0, :].rearrange("p (k e) -> p k e", k=G), ACT.Copy
                  ).then_inc(hot_t_ready, 1)

            def relu_h1(g):
                act.wait_ge(pre_turned, g + 1)
                A(h1[:, :], psum[:, 2, :], ACT.Relu).then_inc(h1_ready, 1)

            def relu_h2(g):
                act.wait_ge(h2_made, g + 1)
                A(h2[:, :, 0:H], psum[:, 3, :].rearrange("p (k h) -> p k h", k=G), ACT.Relu).then_inc(h2_ready, 1)

            def edge_slot(g):
                if not isinstance(g, int) or g < NG:
                    copy_hot_t(g)
                if not isinstance(g, int) or 1 <= g:
                    relu_h1(g - 1)
                    relu_h2(g - 1)

            act.wait_ge(acc_clear, 1)
            edge_slot(0)
            with act.Fori(1, NG) as i:
                edge_slot(i)
            edge_slot(NG)

            def per_block(body):
                with act.Fori(0, NB) as i:
                    body(i)

            def take_turned(k, i, parts, halves):
                act.wait_ge(turned, i + counted("turned", k) + 1)
                act.wait_ge(product, i + counted("product", k))
                A(zt[0:parts, 0:halves * BN].rearrange("p (s c) -> p s c", c=TN),
                  slots(0, halves * BT, TN, parts), ACT.Copy).then_inc(turned_in, 1)

            def rel_hidden(i):
                take_turned(1, i, F, 1)
                act.wait_ge(product, i + counted("product", 1) + 1)
                A(rel_h[:, :, :].rearrange("p q (s c) -> p (q s) c", c=TN), slots(3, 20, TN, 2 * F), ACT.Relu,
                  bias=rel_b1[:, 0:1]).then_inc(stored, 1)

            def to_features(k, i, source, parts, n, func, bias):
                for m in range(n):
                    o = A(feat[0:parts, m, bass.ds(i * BN, BN)].rearrange("p (s c) -> p s c", c=TN),
                          slots(source, n * BT, TN, parts)[:, m * BT:(m + 1) * BT, :], func, bias=bias(m))
                o.then_inc(stored, 1)

            def st2(i):
                take_turned(2, i, F, 1)
                act.wait_ge(product, i + counted("product", 2) + 1)
                to_features(2, i, 3, HALF, 2, ACT.Identity, lambda m: col_in[:, 0, m:m + 1])

            def st4(i):
                take_turned(4, i, HALF, 2)
                act.wait_ge(product, i + counted("product", 4) + 1)
                to_features(4, i, 3, QUART, 4, ACT.Relu, lambda m: bn[0:QUART, m, 5:6])

            def st6(i):
                act.wait_ge(turned, i + counted("turned", 6) + 1)
                to_features(6, i, 0, HALF, 2, ACT.Relu, lambda m: bn[0:HALF, m, 4:5])

            def st8(i):
                act.wait_ge(turned, i + counted("turned", 8) + 1)
                to_features(8, i, 0, F, 1, ACT.Identity, lambda m: col_out[:, 0, 0:1])

            def apply_norm(k, i, parts, n, func, reader, name):
                act.wait_ge(reader, i + counted(name, k))
                for m in range(n):
                    o = A(z[0:parts, m * BN:(m + 1) * BN], feat[0:parts, m, bass.ds(i * BN, BN)], func,
                          scale=bn[0:parts, m, 2:3], bias=bn[0:parts, m, 3:4])
                o.then_inc(prepared, 1)

            def root(n, ap):
                act.wait_ge(var_ready, n)
                A(ap, ap, ACT.Sqrt).then_inc(std_ready, 1)

            per_block(lambda i: take_turned(0, i, H, 1))
            root(1, red[:, 3, :])
            per_block(rel_hidden)
            root(2, red[:, 3, :])
            root(3, deg[:, DINV, :])
            root(4, deg[:, ODINV, :])
            per_block(st2)
            root(5, bn[0:HALF, 0:2, 1:2])
            act.wait_ge(affine, 1)
            per_block(lambda i: apply_norm(3, i, HALF, 2, ACT.Relu, turned, "turned"))
            act.wait_ge(time_act, 2)
            per_block(st4)
            root(6, bn[0:QUART, 0:4, 1:2])
            act.wait_ge(affine, 2)
            per_block(lambda i: apply_norm(5, i, QUART, 4, ACT.Identity, product, "product"))
            per_block(st6)
            root(7, bn[0:HALF, 0:2, 1:2])
            act.wait_ge(affine, 3)
            per_block(lambda i: apply_norm(7, i, HALF, 2, ACT.Identity, product, "product"))
            per_block(st8)
            root(8, bn[0:F, 0:1, 1:2])
            act.wait_ge(affine, 4)
            per_block(lambda i: apply_norm(9, i, F, 1, ACT.Relu, turned, "turned"))
            root(9, red[:, 3, :])
            root(10, red[:, 3, :])

        @block.vector
        def _(dve):
            V = nc.vector
            done = [0]

            def then(ins):
                done[0] += 1
                ins.then_inc(vec_step, 1)
                dve.wait_ge(vec_step, done[0])

            V.memset(rel_w2[:, :, :], 0.0).then_inc(consts_made, 1)
            V.memset(ones_row[:, :], 1.0)
            dve.sem_inc(p_added, 1)
            dve.sem_inc(added, 1)
            dve.sem_inc(stored, 1)
            dve.sem_inc(prepared, 1)
            dve.sem_inc(stored2, 1)
            dve.wait_ge(iota_made, 4)
            V.tensor_copy(iota[:, :], iota_i[:, :])
            then(V.tensor_copy(step_no[:, :], part_i[:, :]))

            def tile_of(o, i, parts_scratch=None):
                then(V.tensor_scalar(o, i, -62.0, 1.0 / TN, ALU.add, ALU.mult))
                then(V.tensor_scalar(o, o, ROUND, None, ALU.add))
                then(V.tensor_scalar(o, o, -ROUND, None, ALU.add))

            dve.wait_ge(ends_in, 48)
            tile_of(first, ends[:, 0, :])
            tile_of(last, ends[:, 1, :])
            then(V.tensor_tensor(mask[0:1, :], last, first, ALU.subtract))
            then(V.tensor_scalar(mask[0:1, :], mask[0:1, :], 1.0, None, ALU.add))
            then(V.tensor_copy(run[:, 0, :], mask[0:1, :]))
            n = 1
            cur = 0
            while n < NC:
                V.tensor_copy(run[:, 1 - cur, 0:n], run[:, cur, 0:n])
                then(V.tensor_tensor(run[:, 1 - cur, n:NC], run[:, cur, n:NC], run[:, cur, 0:NC - n], ALU.add))
                cur = 1 - cur
                n *= 2
            assert cur == 0
            then(V.tensor_tensor(run[:, 0, :], run[:, 0, :], mask[0:1, :], ALU.subtract))
            then(V.tensor_tensor(first, first, run[:, 0, :], ALU.subtract))
            V.tensor_copy(run[:, 1, 0:1], first[:, 0:1])
            V.tensor_tensor(run[:, 1, 1:NC], first[:, 1:NC], first[:, 0:NC - 1], ALU.subtract).then_inc(rows_bc, 1)
            dve.wait_ge(rows_in, 1)
            V.tensor_copy(start_bc[:, :].rearrange("p (b c) -> p b c", b=2), psum[:, 0:2, 0:NC // 2])
            then(V.tensor_copy(jump_bc[:, :].rearrange("p (b c) -> p b c", b=2), psum[:, 2:4, 0:NC // 2]))
            dve.sem_inc(start_copied, 1)
            for j in range(SB):
                then(V.tensor_scalar(mask[:, :], start_bc[:, :], step_no[:, j:j + 1], None, ALU.is_le))
                V.tensor_reduce(cols[:, 0, j:j + 1], mask[:, :], AX.X, ALU.add)
                then(V.tensor_tensor(mask[:, :], mask[:, :], jump_bc[:, :], ALU.mult))
                then(V.tensor_reduce(cols[:, 1, j:j + 1], mask[:, :], AX.X, ALU.add))
            then(V.tensor_tensor(cols[:, 2, :], cols[:, 1, :], step_no[:, :], ALU.add))
            V.tensor_scalar(cols[:, 3, :], cols[:, 2, :], float(TN), None, ALU.mult)
            V.tensor_scalar(cols_i[:, 0, :], cols[:, 2, :], float(NT - 1), None, ALU.min)
            then(V.tensor_scalar(cols_i[:, 1, :], cols[:, 0, :], -1.0, None, ALU.add))
            dve.sem_inc(step_idx, 1)

            for j in range(SB):
                dve.wait_ge(step_in[j % 2], 64 * (j // 2 + 1))
                if j:
                    dve.wait_ge(turned_rows, j)
                e = step_e[:, j % 2]
                V.tensor_scalar(step_f[:, 0, :], e[:, 0, :], cols[:, 3, j:j + 1], None, ALU.subtract)
                V.tensor_copy(step_f[:, 1, :], e[:, 1, :])
                V.scalar_tensor_tensor(step_f[:, 2, :], e[:, 1, :], float(NR), e[:, 2, :], ALU.mult, ALU.add)
                V.tensor_copy(step_f[:, 3, :], e[:, 3, :].bitcast(F32))
                tile_of(step_f[:, 5, :], e[:, 1, :])
                then(V.scalar_tensor_tensor(step_f[:, 4, :], step_f[:, 5, :], -float(TN), e[:, 1, :],
                                            ALU.mult, ALU.add))
                then(V.tensor_scalar(mask[:, 0:CE], step_f[:, 0, :], 0.0, None, ALU.is_ge))
                then(V.scalar_tensor_tensor(mask[:, 0:CE], step_f[:, 0, :], float(TN - 1), mask[:, 0:CE],
                                            ALU.is_le, ALU.mult))
                then(V.scalar_tensor_tensor(step_f[:, 5, :], step_f[:, 5, :], 1.0, mask[:, 0:CE],
                                            ALU.add, ALU.mult))
                dve.sem_inc(turn_rows, 1)
                dve.wait_ge(turned_rows, j + 1)
                c = slice(j * CE, (j + 1) * CE)
                V.tensor_copy(dst_rel[:, c], psum[:, 0, 0:CE])
                V.tensor_copy(src_idx[:, c], psum[:, 0, CE:2 * CE])
                V.tensor_copy(rel_idx[:, c], psum[:, 0, 2 * CE:3 * CE])
                V.tensor_copy(wgt[:, c], psum[:, 0, 3 * CE:4 * CE])
                V.tensor_copy(src_lo[:, c], psum[:, 1, 0:CE])
                V.tensor_copy(src_hi[:, c], psum[:, 1, CE:2 * CE]).then_inc(tables_made, 1)
            dve.wait_ge(tables_made, SB)

            dve.wait_ge(weights_in, 16 * N_LOADS)
            for i in range(NB):
                dve.wait_ge(node_prod, i + 1)
                dve.wait_ge(src_half, i + 1)
                V.tensor_tensor(dst_half_sb[:, i * BT:(i + 1) * BT, :], psum[0:TN, 0:BT, H:2 * H],
                                b1[:, :].unsqueeze(1).to_broadcast([TN, BT, H]), ALU.add).then_inc(dst_half, 1)
            dve.wait_ge(dst_half, NB)

            tc = [time_col[:, c:c + 1] for c in range(12)]
            then(V.tensor_tensor(tc[7], tc[0], tc[2], ALU.mult))
            then(V.scalar_tensor_tensor(tc[8], tc[7], 1.0 / (2 * np.pi), tc[1], ALU.mult, ALU.add))
            then(V.tensor_scalar(tc[8], tc[8], ROUND, None, ALU.add))
            then(V.tensor_scalar(tc[8], tc[8], -ROUND, None, ALU.add))
            for part in TWO_PI:
                then(V.scalar_tensor_tensor(tc[7], tc[8], -part, tc[7], ALU.mult, ALU.add))
            then(V.scalar_tensor_tensor(tc[7], tc[1], 2 * np.pi, tc[7], ALU.mult, ALU.add))
            V.tensor_scalar(tc[6], tc[7], -3.1415925, 3.1415925, ALU.max, ALU.min).then_inc(time_emb, 1)

            def make_hot(g, u, sem_, weighted=False):
                for k in range(G):
                    s = g * G + k
                    if weighted:
                        o = V.tensor_scalar(hot[:, u, k, :], iota[:, 0:TN], dst_rel[:, bass.ds(s, 1)],
                                            wgt[:, bass.ds(s, 1)], ALU.is_equal, ALU.mult)
                    else:
                        o = V.tensor_scalar(hot[:, u, k, :], iota[:, 0:TN], dst_rel[:, bass.ds(s, 1)], None,
                                            ALU.is_equal)
                o.then_inc(sem_, 1)

            def take_idx(g, u, tab, sem_):
                V.tensor_copy(idx[:, u, :], tab[:, bass.ds(g * G, G)]).then_inc(sem_, 1)

            def add_group(g, banks, width, pitch, sem_, base):
                _, tile = nc.values_load_multi_w_load_instructions(
                    step_regs[0:1, 0, bass.ds(g * G, G)], engines=[dve.engine], min_val=0, max_val=NT - 1,
                    skip_runtime_bounds_check_because="the table is clamped to the tiles")
                for k in range(G):
                    dve.wait_ge(sem_, g * G + (base + k))
                    t = acc[:, bass.ds(tile[k], 1), 0:width].rearrange("p a f -> p (a f)")
                    c = (k % 2) * pitch
                    V.tensor_tensor(t, t, psum[0:TN, banks + k // 2, c:c + width], ALU.add).then_inc(sem_, 1)

            V.memset(h2[:, :, H:H + 1], 1.0)
            then(V.memset(acc[:, :, :], 0.0))
            dve.sem_inc(acc_clear, 1)
            dve.wait_ge(regs_in, 16)
            for g in range(3):
                take_idx(g, g, src_idx, idx_ready)
            make_hot(0, 0, hot_ready)

            def edge_slot(g, u, n):
                static = isinstance(g, int)
                if not static or g >= 3:
                    dve.wait_ge(spread, g - 1 if static else g - 1)
                    add_group(g - 3, 4 + 2 * ((u - 3) % 2), H + 1, H + 1, added, 1)
                if not static or g + 3 < NG:
                    take_idx(g + 3, (u + 3) % RING, src_idx, idx_ready)
                if not static or g + 1 < NG:
                    make_hot(g + 1, (u + 1) % RING, hot_ready)
                if not static or g < NG:
                    dve.wait_ge(edge_sum, g + 1)
                    dve.wait_ge(gathered[u], n)
                    V.tensor_tensor(pre[:, :, :], psum[:, 1, :].rearrange("p (k h) -> p k h", k=G),
                                    rows[:, u, :, 0:H], ALU.add).then_inc(edge_pre, 1)

            for g in range(RING):
                edge_slot(g, g, 16 * G)
            with dve.Fori(1, NG // RING - 1) as i:
                for u in range(RING):
                    edge_slot(i * RING + u, u, (i + 1) * (16 * G))
            for g in range(NG - RING, NG + 3):
                edge_slot(g, g % RING, 16 * G * (g // RING + 1))
            dve.wait_ge(added, G * NG + 1)

            def per_block(body):
                with dve.Fori(0, NB) as i:
                    body(i)

            def blk(t, i, f0, f1):
                return t[0:TN, bass.ds(i * BT, BT), f0:f1]

            def zb(width):
                return z[0:TN, 0:BT * width].rearrange("p (u f) -> p u f", u=BT)

            def layer_norm(o, x, n):
                then(V.tensor_reduce(red[:, 0, :], x[:, :, :], AX.X, ALU.add))
                then(V.tensor_scalar(red[:, 0, :], red[:, 0, :], 1.0 / F, None, ALU.mult))
                then(V.tensor_tensor(x[:, :, :], x[:, :, :], bcast(red[:, 0, :], NT, F), ALU.subtract))
                then(V.tensor_tensor(scratch[:, :, :], x[:, :, :], x[:, :, :], ALU.mult))
                then(V.tensor_reduce(red[:, 2, :], scratch[:, :, :], AX.X, ALU.add))
                V.tensor_scalar(red[:, 3, :], red[:, 2, :], 1.0 / F, EPS, ALU.mult, ALU.add).then_inc(var_ready, 1)
                dve.wait_ge(std_ready, n)
                then(V.reciprocal(red[:, 4, :], red[:, 3, :]))
                then(V.tensor_tensor(o[:, :, :], x[:, :, :], bcast(red[:, 4, :], NT, F), ALU.mult))

            def conv_sum(width):
                then(V.tensor_tensor(table[0:TN, :, 0:width], table[0:TN, :, 0:width], acc[:, :, 0:width], ALU.add))

            def prepare(k, i, width, src, scale):
                dve.wait_ge(turned, i + counted("turned", k))
                if scale is None:
                    o = V.tensor_copy(zb(width), blk(src, i, 0, width))
                else:
                    o = V.tensor_tensor(zb(width), blk(src, i, 0, width),
                                        bcast(deg[:, scale, bass.ds(i * BT, BT)], BT, width), ALU.mult)
                o.then_inc(prepared, 1)

            def add_stats(k, i, parts, n):
                dve.wait_ge(stored, i + counted("stored", k) + 1)
                for m in range(n):
                    for c, (c0, cn) in enumerate(((0, 313), (313, 312))):
                        o = V.bn_stats(stats[0:parts, m, bass.ds(i, 1), c, :].rearrange("p a b -> p (a b)"),
                                       feat[0:parts, m, bass.ds(i * BN + c0, cn)])
                o.then_inc(stats_made, 1)

            def norm_affine(k, n, parts, m_parts, gain, shift):
                dve.wait_ge(stats_made, NB * (k + 1))
                for m in range(m_parts):
                    last_ = V.bn_aggr(bn[0:parts, m, 0:2],
                                      stats[0:parts, m, :, :, :].rearrange("p b c s -> p (b c s)"))
                then(last_)
                V.tensor_scalar(bn[0:parts, 0:m_parts, 1:2], bn[0:parts, 0:m_parts, 1:2], EPS, None, ALU.add
                                ).then_inc(var_ready, 1)
                dve.wait_ge(std_ready, n)
                b = [bn[0:parts, 0:m_parts, c] for c in range(8)]
                then(V.reciprocal(b[2], b[1]))
                then(V.tensor_tensor(b[2], b[2], gain, ALU.mult))
                then(V.tensor_tensor(b[3], b[0], b[2], ALU.mult))
                then(V.tensor_tensor(b[3], shift, b[3], ALU.subtract))
                dve.sem_inc(affine, 1)

            def to_table(k, i, source, name, width, bank=0):
                dve.wait_ge(source, i + counted(name, k) + 1)
                V.tensor_tensor(blk(table, i, 0, width), wide(bank, BT, width),
                                bcast(deg[:, DINV, bass.ds(i * BT, BT)], BT, width), ALU.mult).then_inc(stored, 1)

            def one_pass(k, width, weighted):
                then(V.memset(acc[:, :, 0:width], 0.0))
                tab = rel_idx if weighted else src_idx

                def sources(g, u):
                    if not weighted:
                        return
                    for s in range(G):
                        V.tensor_scalar(lo_hot[:, u % 2, s, :], iota[:, 0:TN], src_lo[:, bass.ds(g * G + s, 1)],
                                        None, ALU.is_equal)
                        V.tensor_scalar(hi_hot[:, u % 2, s, :], iota[:, 1:NT + 1], src_hi[:, bass.ds(g * G + s, 1)],
                                        None, ALU.is_equal)

                def slot(g, u):
                    static = isinstance(g, int)
                    if not static or g >= 1:
                        dve.wait_ge(p_sum, g + (NG * k + 1))
                        add_group(g - 1, 2 * ((u - 1) % 2), width, C3, p_added, G * NG * k + 1)
                    if not static or g + 3 < NG:
                        take_idx(g + 3, (u + 3) % RING, tab, p_idx)
                    if not static or g + 1 < NG:
                        sources(g + 1, u + 1)
                        make_hot(g + 1, (u + 1) % RING, p_hot, weighted)

                for g in range(3):
                    take_idx(g, g, tab, p_idx)
                sources(0, 0)
                make_hot(0, 0, p_hot, weighted)
                for g in range(RING):
                    slot(g, g)
                with dve.Fori(1, NG // RING - 1) as i:
                    for u in range(RING):
                        slot(i * RING + u, u)
                for g in range(NG - RING, NG + 1):
                    slot(g, g % RING)
                dve.wait_ge(p_added, G * NG * (k + 1) + 1)

            V.tensor_copy(deg[:, CNT, :], acc[:, :, H])
            then(V.tensor_scalar(deg[:, RCNT, :], acc[:, :, H], 1.0, None, ALU.max))
            then(V.reciprocal(deg[:, RCNT, :], deg[:, RCNT, :]))
            then(V.tensor_tensor(deg[:, BSCALE, :], deg[:, RCNT, :], deg[:, CNT, :], ALU.mult))

            def st0(i):
                prepare(0, i, H, acc, RCNT)
                dve.wait_ge(product, i + counted("product", 0) + 1)
                V.tensor_copy(y[:, bass.ds(i * BT, BT), :], psum[0:TN, 3, 0:BT * F].rearrange("p (u f) -> p u f", u=BT)
                              ).then_inc(stored, 1)

            per_block(st0)
            dve.wait_ge(stored, counted("stored", 1))
            then(V.tensor_tensor(scratch[:, :, :], b3[:, :].unsqueeze(1).to_broadcast([TN, NT, F]),
                                 bcast(deg[:, BSCALE, :], NT, F), ALU.mult))
            then(V.tensor_tensor(y[:, :, :], y[:, :, :], scratch[:, :, :], ALU.add))
            then(V.tensor_tensor(y[:, :, :], y[:, :, :], x0[:, :, :], ALU.add))
            then(V.tensor_tensor(y[:, :, :], y[:, :, :], x0[:, :, :], ALU.add))
            layer_norm(x_cur, y, 1)

            for i in range(NB):
                prepare(1, i, F, x_cur, None)
                dve.wait_ge(product2, i + 2)
                if i:
                    dve.wait_ge(table_out, 16 * i)
                V.tensor_copy(rel_out[:, :, :], psum[0:TN, 3:8, 0:NR * F]).then_inc(stored2, 1)

            one_pass(0, *PASSES[0])
            V.tensor_scalar(deg[:, ODINV, :], psum[0:TN, 6, 0:NT], 1.0, None, ALU.add)
            V.tensor_scalar(deg[:, DINV, :], deg[:, CNT, :], 1.0, None, ALU.add)
            then(V.tensor_tensor(y[:, :, :], acc[:, :, 0:F], rel_b2[:, :].unsqueeze(1).to_broadcast([TN, NT, F]),
                                 ALU.add))
            then(V.tensor_scalar(y[:, :, :], y[:, :, :], 0.0, None, ALU.max))
            then(V.tensor_tensor(y[:, :, :], y[:, :, :], x_cur[:, :, :], ALU.add))
            layer_norm(x_cur, y, 2)
            dve.sem_inc(var_ready, 2)
            dve.wait_ge(std_ready, 4)
            V.reciprocal(deg[:, ODINV, :], deg[:, ODINV, :])
            then(V.reciprocal(deg[:, DINV, :], deg[:, DINV, :]))
            then(V.tensor_tensor(table[0:TN, :, 0:F], x_cur[:, :, :], bcast(deg[:, DINV, :], NT, F), ALU.mult))
            dve.sem_inc(table_ready, 1)

            one_pass(1, *PASSES[1])
            conv_sum(F)

            def conv_in(k, width, parts, n):
                def body(i):
                    prepare(k, i, width, table, DINV)
                    add_stats(k, i, parts, n)
                per_block(body)

            conv_in(2, F, HALF, 2)
            norm_affine(0, 5, HALF, 2, col_in[:, 1, :], col_in[:, 2, :])
            per_block(lambda i: to_table(3, i, turned, "turned", C3))
            dve.wait_ge(stored, counted("stored", 4))
            dve.sem_inc(table_ready, 1)
            one_pass(2, *PASSES[2])
            conv_sum(C3)
            dve.wait_ge(time_act, 2)
            V.tensor_tensor(bn[0:QUART, :, 5], bn[0:QUART, :, 7], col_1[:, 0, :], ALU.add)
            then(V.tensor_tensor(bn[0:HALF, 0:2, 4], bn[0:HALF, 0:2, 6], col_2[:, 0, :], ALU.add))
            conv_in(4, C3, QUART, 4)
            norm_affine(1, 6, QUART, 4, col_1[:, 1, :], col_1[:, 2, :])
            per_block(lambda i: to_table(5, i, product, "product", C3))
            dve.wait_ge(stored, counted("stored", 6))
            dve.sem_inc(table_ready, 1)
            one_pass(3, *PASSES[3])
            conv_sum(C3)
            conv_in(6, C3, HALF, 2)
            norm_affine(2, 7, HALF, 2, col_2[:, 1, :], col_2[:, 2, :])
            per_block(lambda i: to_table(7, i, product, "product", F))
            dve.wait_ge(stored, counted("stored", 8))
            dve.sem_inc(table_ready, 1)
            one_pass(4, *PASSES[4])
            conv_sum(F)
            conv_in(8, F, F, 1)
            norm_affine(3, 8, F, 1, col_out[:, 1, :], col_out[:, 2, :])

            def st9(i):
                dve.wait_ge(turned, i + counted("turned", 9) + 1)
                V.tensor_copy(blk(y, i, 0, F), wide(0, BT, F)).then_inc(stored, 1)

            per_block(st9)
            dve.wait_ge(stored, 1 + NB * 10)
            then(V.tensor_tensor(y[:, :, :], y[:, :, :], x_cur[:, :, :], ALU.add))
            layer_norm(x_cur, y, 9)
            then(V.tensor_tensor(table[0:TN, :, 0:F], x_cur[:, :, :], bcast(deg[:, ODINV, :], NT, F), ALU.mult))
            dve.sem_inc(table_ready, 1)
            one_pass(5, *PASSES[5])
            conv_sum(F)
            then(V.tensor_tensor(y[:, :, :], table[0:TN, :, 0:F], bcast(deg[:, ODINV, :], NT, F), ALU.mult))
            then(V.tensor_tensor(x0[:, :, :], y[:, :, :], x_cur[:, :, :], ALU.add))
            layer_norm(y, x0, 10)
            dve.sem_inc(result, 1)


def two_pi_parts():
    p = 2 * np.pi
    one = 6.28125
    two = float(np.round((p - one) * 2.0 ** 21) / 2.0 ** 21)
    return one, two, float(np.float32(p - one - two))


TWO_PI = two_pi_parts()
N_LOADS = 22 + 14 + 8


def kernel(**inputs):
    import concourse.bacc as _bacc
    from concourse.bass_utils import run_bass_kernel_spmd as _run

    nc = _bacc.Bacc("TRN2", target_bir_lowering=False, num_devices=1)

    def chunked(v, fill):
        v = np.ascontiguousarray(v).reshape(-1)
        o = np.full((NC * CE,), fill, v.dtype)
        o[:E] = v
        return o.reshape(NC, CE)

    attr_t = np.zeros((16, NC * CE), np.float32)
    attr_t[:, :E] = np.asarray(inputs["edge_attr_16"]).T
    half = H // 2
    freqs = np.exp(np.arange(half, dtype=np.float32) * np.float32(-np.log(10000.0) / (half - 1))).astype(np.float32)
    phase = np.repeat(np.array([0.0, 0.25], np.float32), half)
    feeds = {
        "x": inputs["x"], "xT": np.asarray(inputs["x"]).T,
        "dst": chunked(inputs["dst"], PADDED_DST), "src": chunked(inputs["src"], 0),
        "type": chunked(inputs["edge_type_8"], 0), "w": chunked(inputs["edge_weight1"], 0), "attrT": attr_t,
        "W1": inputs["L0_gnn_W1"], "b1": inputs["L0_gnn_b1"], "W2": inputs["L0_gnn_W2"], "b2": inputs["L0_gnn_b2"],
        "W3": inputs["L0_gnn_W3"], "b3": inputs["L0_gnn_b3"],
        "rw1": inputs["L1_gnn_weight1"], "rw2": inputs["L1_gnn_weight2"], "rb1": inputs["L1_gnn_bias1"],
        "rb2": inputs["L1_gnn_bias2"],
        "timestep": inputs["L2_gnn_timestep"],
        "time_const": np.stack([np.concatenate([freqs, freqs]), phase], axis=1),
    }
    for name in ("Wtm", "btm", "W_in", "b_in", "g_in", "be_in", "Wt1", "bt1", "Wc1", "bc1", "g1", "be1", "Wt2",
                 "bt2", "Wc2", "bc2", "g2", "be2", "W_out", "b_out", "g_out", "be_out"):
        feeds[name] = inputs["L2_gnn_" + name]
    arrays, aps = {}, {}
    for name, v in feeds.items():
        v = np.ascontiguousarray(v)
        arrays[f"in_{name}_dram"] = v
        aps[name] = nc.dram_tensor(f"in_{name}_dram", v.shape, mybir.dt.from_np(v.dtype), kind="ExternalInput").ap()
    out = nc.dram_tensor("out_0_dram", (N, F), F32, kind="ExternalOutput").ap()
    build(nc, aps, out)
    r = _run(nc, [arrays], core_ids=[0])
    return r.results[0]["out_0_dram"]
```
